# Optimizing a Trainium2 kernel written in Bass

```python
import numpy as np
import jax
import jax.numpy as jnp

def _softmax(x, axis=-1):
    return jax.nn.softmax(x, axis=axis)
def _gelu(x):
    return jax.nn.gelu(x, approximate=True)
def _silu(x):
    return jax.nn.silu(x)
def _sigmoid(x):
    return jax.nn.sigmoid(x)
def _layernorm(x, axis=-1, eps=1e-5):
    m = jnp.mean(x, axis=axis, keepdims=True)
    v = jnp.var(x, axis=axis, keepdims=True)
    return (x - m) / jnp.sqrt(v + eps)
def _scatter_add(tgt, idx, src, axis=0):
    return tgt.at[idx].add(src)
def _segment_sum(src, seg, n):
    return jax.ops.segment_sum(src, seg, n)

kernel_name = 'mk_conv_seq_d1_conv_nhwc768_1b4fcf'

def setup_inputs(seed: int = 0):
    np.random.seed(seed)
    _w = jnp.asarray
    def _rec_inputs():
        import jax
        import jax.numpy as jnp
        _gk = jax.random.key(seed)
        x = -4.65e-05 + 0.9999 * jax.random.normal(jax.random.fold_in(_gk, 1), (4, 128, 128, 768), jnp.float32)
        return x
    x = _rec_inputs()
    def _L0_conv_setup():
        import jax, jax.numpy as jnp
        import numpy as np
        HIDDEN = 768
        NUM_BLOCKS = 8
        BLOCK = HIDDEN // NUM_BLOCKS
        FACTOR = 1
        LAMBDA = 0.01
        SCALE = 0.02

        def _softshrink(v, lam):
            return jnp.sign(v) * jnp.maximum(jnp.abs(v) - lam, 0.0)
        key = jax.random.key(seed)
        k0, k1, k2, k3, k4 = jax.random.split(key, 5)
        B, H, W, C = (4, 128, 128, HIDDEN)
        x = jax.random.normal(k0, (B, H, W, C), dtype=jnp.float32)
        w1 = SCALE * jax.random.normal(k1, (2, NUM_BLOCKS, BLOCK, BLOCK * FACTOR), dtype=jnp.float32)
        b1 = SCALE * jax.random.normal(k2, (2, NUM_BLOCKS, BLOCK * FACTOR), dtype=jnp.float32)
        w2 = SCALE * jax.random.normal(k3, (2, NUM_BLOCKS, BLOCK * FACTOR, BLOCK), dtype=jnp.float32)
        b2 = SCALE * jax.random.normal(k4, (2, NUM_BLOCKS, BLOCK), dtype=jnp.float32)
        return {'x': x, 'w1': w1, 'b1': b1, 'w2': w2, 'b2': b2}
    _L0_conv_all = _L0_conv_setup()
    _L0_conv_in = {k: v for k, v in _L0_conv_all.items() if k in ('w1', 'b1', 'w2', 'b2', )}
    del _L0_conv_all

    return {
        "x": x,
        "L0_conv_w1": _L0_conv_in["w1"],
        "L0_conv_b1": _L0_conv_in["b1"],
        "L0_conv_w2": _L0_conv_in["w2"],
        "L0_conv_b2": _L0_conv_in["b2"],
    }

def reference(x, L0_conv_w1, L0_conv_b1, L0_conv_w2, L0_conv_b2):
    import jax
    import jax.numpy as jnp
    def _L0_conv_ref(x, w1, b1, w2, b2):
        import jax, jax.numpy as jnp
        import numpy as np
        HIDDEN = 768
        NUM_BLOCKS = 8
        BLOCK = HIDDEN // NUM_BLOCKS
        FACTOR = 1
        LAMBDA = 0.01
        SCALE = 0.02

        def _softshrink(v, lam):
            return jnp.sign(v) * jnp.maximum(jnp.abs(v) - lam, 0.0)
        bias = x
        dtype = x.dtype
        B, H, W, C = x.shape
        xf = jnp.fft.rfft2(x.astype(jnp.float32), axes=(1, 2), norm='ortho')
        xf = xf.reshape(B, H, W // 2 + 1, NUM_BLOCKS, BLOCK)
        xr, xi = (xf.real, xf.imag)
        o1r = jax.nn.relu(jnp.einsum('bhwni,nio->bhwno', xr, w1[0]) - jnp.einsum('bhwni,nio->bhwno', xi, w1[1]) + b1[0])
        o1i = jax.nn.relu(jnp.einsum('bhwni,nio->bhwno', xi, w1[0]) + jnp.einsum('bhwni,nio->bhwno', xr, w1[1]) + b1[1])
        o2r = jnp.einsum('bhwni,nio->bhwno', o1r, w2[0]) - jnp.einsum('bhwni,nio->bhwno', o1i, w2[1]) + b2[0]
        o2i = jnp.einsum('bhwni,nio->bhwno', o1i, w2[0]) + jnp.einsum('bhwni,nio->bhwno', o1r, w2[1]) + b2[1]
        o = jnp.stack([o2r, o2i], axis=-1)
        o = _softshrink(o, LAMBDA)
        xc = jax.lax.complex(o[..., 0], o[..., 1]).reshape(B, H, W // 2 + 1, C)
        out = jnp.fft.irfft2(xc, s=(H, W), axes=(1, 2), norm='ortho')
        return out.astype(dtype) + bias

    def _gn(v, G=32, eps=1e-5):
        B_, H_, W_, C_ = v.shape
        g = v.reshape(B_, H_, W_, G, C_ // G)
        m = jnp.mean(g, axis=(1, 2, 4), keepdims=True)
        s = jnp.var(g, axis=(1, 2, 4), keepdims=True)
        return ((g - m) / jnp.sqrt(s + eps)).reshape(v.shape)

    def _ln_c(v, eps=1e-6):
        m = jnp.mean(v, axis=-1, keepdims=True)
        s = jnp.var(v, axis=-1, keepdims=True)
        return (v - m) / jnp.sqrt(s + eps)

    def _ln_t(v, eps=1e-5):
        m = jnp.mean(v, axis=-1, keepdims=True)
        s = jnp.var(v, axis=-1, keepdims=True)
        return (v - m) / jnp.sqrt(s + eps)

    def _to_tokens(v):
        B_, H_, W_, C_ = v.shape
        return v.reshape(B_, H_ * W_, C_)
    def _from_tokens(t, like):
        return t.reshape(like.shape)

    x = _L0_conv_ref(x, L0_conv_w1, L0_conv_b1, L0_conv_w2, L0_conv_b2)
    return x


_drawn_inputs = setup_inputs


def setup_inputs(seed=0):
    import zlib

    import numpy as np

    out = dict(_drawn_inputs(seed))
    spreads = {}
    factors = {'L0_conv_b1': 8.0}
    for name, (base, spread) in spreads.items():
        noise = np.random.default_rng([zlib.crc32(name.encode()), seed]).standard_normal(out[name].shape)
        drawn = base * np.exp(spread * noise) if base else spread * noise
        out[name] = jnp.asarray(drawn.astype(out[name].dtype))
    for name, factor in factors.items():
        out[name] = (out[name] * factor).astype(out[name].dtype)
    return out
```

```python
from contextlib import ExitStack

import numpy as np

import concourse.bass as bass
from concourse import mybir

F32 = mybir.dt.float32
ALU = mybir.AluOpType
ACT = mybir.ActivationFunctionType

IMAGES, SIZE, HIDDEN, BLOCKS = 4, 128, 768, 8
BLOCK = HIDDEN // BLOCKS
UNITS = IMAGES * BLOCKS
HALF = SIZE // 2
LAMBDA = 0.01

FW_EVEN, FW_ODD, FH, IH, IW_COS, IW_SIN, FLIP_RE, FLIP_IM = (slice(SIZE * i, SIZE * (i + 1)) for i in range(8))

STEPS = [(0, HALF)] + [(k, k + 1) for k in range(1, HALF - 1, 2)] + [(HALF - 1,)]
NS = len(STEPS)
FLIP_AT = 6

A_SLOTS = 4
NA = SIZE // A_SLOTS
E_CHANNELS = 4
NE = BLOCK // E_CHANNELS
CHUNK = 12
NQ = BLOCK // CHUNK
EQ = CHUNK // E_CHANNELS
F_CHANNELS = 6
FQ = 2 * (CHUNK // F_CHANNELS)
NF = NQ * FQ
PIECES = [(1, 16), (17, 32), (33, 48), (49, 63)]
ROWS = [[(0, 17), (112, 128)], [(17, 33), (96, 112)], [(33, 49), (80, 96)], [(49, 80)]]
NROWS = sum(map(len, ROWS))
FOLDS = len(PIECES) + 1


def constants():
    k = np.arange(SIZE)
    cos = np.cos(2 * np.pi * np.outer(k, k) / SIZE)
    sin = np.sin(2 * np.pi * np.outer(k, k) / SIZE)
    kw = np.arange(1, HALF)
    even = np.zeros((SIZE, SIZE))
    even[:, 0], even[:, 1] = cos[:, 0], cos[:, HALF]
    even[:, 2::2], even[:, 3::2] = cos[:, kw], -sin[:, kw]
    odd = np.zeros((SIZE, SIZE))
    odd[:, 0:-2:2], odd[:, 1:-2:2] = sin[:, kw], cos[:, kw]
    odd[:, -2], odd[:, -1] = cos[:, 0], cos[:, HALF]
    fh = np.concatenate([cos[:HALF + 1], sin[HALF + 1:]])
    fh[[0, HALF]] /= 2
    ih = np.concatenate([cos[:, :HALF + 1], -sin[:, HALF + 1:]], axis=1)
    iw_cos, iw_sin = np.zeros((SIZE, SIZE)), np.zeros((SIZE, SIZE))
    iw_cos[0], iw_cos[1] = cos[0], cos[HALF]
    iw_sin[0], iw_sin[1] = -cos[0], -cos[HALF]
    iw_cos[2::2], iw_cos[3::2] = 2 * cos[kw], -2 * sin[kw]
    iw_sin[2::2], iw_sin[3::2] = -2 * sin[kw], -2 * cos[kw]
    flip = np.eye(SIZE)[(-k) % SIZE]
    scale = 1.0 / SIZE
    parts = [even * scale, odd * scale, fh, ih, iw_cos * scale, iw_sin * scale,
             (np.eye(SIZE) + flip) / 2, (np.eye(SIZE) - flip) / 2]
    return np.concatenate(parts, axis=1).astype(np.float32)


def fourier_mlp(nc, x, w1, b1, w2, b2, dft, out):
    with ExitStack() as ctx:
        def sb(name, shape):
            return ctx.enter_context(nc.sbuf_tensor(name, shape, F32))

        def sem(name):
            return ctx.enter_context(nc.semaphore(name))

        xs = [sb(f"x{i}", [SIZE, SIZE, BLOCK]) for i in range(2)]
        spectrum = sb("spectrum", [SIZE, (SIZE + 2) * SIZE])
        U = spectrum[:, :].rearrange("p (j s) -> p j s", s=SIZE)
        mixed = [sb(f"mixed{i}", [SIZE, 2, 2 * BLOCK]) for i in range(2)]
        hidden = [sb(f"hidden{i}", [BLOCK + 1, 2, 2, SIZE]) for i in range(2)]
        clipped = [sb(f"clipped{i}", [SIZE, 4, BLOCK]) for i in range(2)]
        real_kw = sb("real_kw", [SIZE, 4, BLOCK])
        sums = [sb(f"sums{i}", [SIZE, CHUNK, SIZE]) for i in range(2)]
        doubled = sb("doubled", [SIZE, PIECES[0][1], BLOCK])
        mats = sb("mats", [SIZE, 8 * SIZE])
        w1t = [sb(f"w1t{i}", [BLOCK, 3 * BLOCK]) for i in range(2)]
        w2t = [sb(f"w2t{i}", [BLOCK + 1, 3 * BLOCK]) for i in range(2)]
        b1t = [sb(f"b1t{i}", [BLOCK, 2]) for i in range(2)]
        psum = ctx.enter_context(nc.psum_tensor("psum", [SIZE, 8, 512], F32))

        def bank(i, p=SIZE, n=512):
            return psum[0:p, i, 0:n]

        def bank_a(g):
            return bank(4 + g % 4, BLOCK)

        def bank_b(s):
            return bank(s % 2, SIZE, 4 * BLOCK).rearrange("p (k y) -> p k y", k=2)

        def bank_c(s):
            return bank(2 + s % 2, BLOCK).rearrange("p (r k y) -> p r k y", r=2, k=2)

        def bank_d(s):
            return bank(4 + s % 2, SIZE, 4 * BLOCK).rearrange("p (k y) -> p k y", k=2)

        bank_flip = bank(6, SIZE, 2 * BLOCK).rearrange("p (k c) -> p k c", k=2)

        def bank_e(e):
            return bank(4 + e % 4)

        def bank_f(j):
            rows = HALF + 1 if j < FQ // 2 else HALF - 1
            return bank(j, SIZE, F_CHANNELS * rows).rearrange("p (c h) -> p c h", h=rows)

        x_loaded = [sem(f"x_loaded{i}") for i in range(2)]
        x_folded = [sem(f"x_folded{i}") for i in range(2)]
        x_stored = [sem(f"x_stored{i}") for i in range(2)]
        w_loaded = [sem(f"w_loaded{i}") for i in range(2)]
        mats_loaded = sem("mats_loaded")
        ones_set = sem("ones_set")
        w_negated = sem("w_negated")
        u_zeroed = sem("u_zeroed")
        a_done, a_copied = sem("a_done"), sem("a_copied")
        b_done, b_copied = sem("b_done"), sem("b_copied")
        c_done, relu_done = sem("c_done"), sem("relu_done")
        d_done, clip_done, shrunk = sem("d_done"), sem("clip_done"), sem("shrunk")
        flip_done, flip_copied = sem("flip_done"), sem("flip_copied")
        e_done, e_copied = sem("e_done"), sem("e_copied")
        f_done, f_added = sem("f_done"), sem("f_added")
        pool_steps, dve_sums = sem("pool_steps"), sem("dve_sums")
        unfold_even, unfolded = sem("unfold_even"), sem("unfolded")

        block = ctx.enter_context(nc.Block())

        PAIRS = UNITS // 2
        PER_IMAGE = BLOCKS // 2

        def channels(m, par):
            return bass.ds((m % PER_IMAGE) * (2 * BLOCK) + par * BLOCK, BLOCK)

        def pixels(t, m, par):
            return t[m // PER_IMAGE].rearrange("h w c -> w h c")[:, :, channels(m, par)]

        def mirrored(t, lo, hi):
            return t[:, SIZE - hi:SIZE - lo + 1, :][:, ::-1, :]

        @block.sync
        def _(sp):
            def load(m, par):
                blk = (m % PER_IMAGE) * 2 + par
                pair = "r i o -> i r o"
                sp.dma_start(w1t[par][:, BLOCK:].rearrange("p (r o) -> p r o", r=2),
                             w1[:, blk].rearrange(pair)).then_inc(w_loaded[par], 16)
                sp.dma_start(w2t[par][0:BLOCK, BLOCK:].rearrange("p (r o) -> p r o", r=2),
                             w2[:, blk].rearrange(pair)).then_inc(w_loaded[par], 16)
                sp.dma_start(w2t[par][BLOCK:BLOCK + 1, BLOCK:].rearrange("p (r o) -> p r o", r=2),
                             b2[:, bass.ds(blk, 1)].rearrange("r n o -> n r o")).then_inc(w_loaded[par], 16)
                with nc.allow_non_contiguous_dma(reason="96 pairs of biases"):
                    sp.dma_start(b1t[par][:, :], b1[:, blk].rearrange("r o -> o r")).then_inc(w_loaded[par], 16)
                src = pixels(x, m, par)
                for rows in ROWS:
                    for lo, hi in rows:
                        sp.dma_start(xs[par][:, lo:hi, :], src[:, lo:hi, :]).then_inc(x_loaded[par], 16)

            def store(m, par):
                dst = pixels(out, m, par)
                for i, rows in enumerate(ROWS):
                    sp.wait_ge(unfolded, (m * 2 + par) * len(PIECES) + i + 1)
                    for lo, hi in rows:
                        sp.dma_start(dst[:, lo:hi, :], xs[par][:, lo:hi, :]).then_inc(x_stored[par], 16)

            load(0, 0)
            sp.dma_start(mats[:, :], dft).then_inc(mats_loaded, 16)
            load(0, 1)
            with sp.Fori(0, PAIRS - 1) as m:
                for par in range(2):
                    store(m, par)
                    sp.wait_ge(x_stored[par], (m + 1) * (16 * NROWS))
                    load(m + 1, par)
            for par in range(2):
                store(PAIRS - 1, par)
            for par in range(2):
                sp.wait_ge(x_stored[par], PAIRS * 16 * NROWS)

        @block.gpsimd
        def _(pool):
            def fold(m, par):
                t = xs[par]
                steps = (m * 2 + par - 1) * (2 * len(PIECES))
                pool.wait_ge(x_loaded[par], (m + 1) * (16 * NROWS))
                both = t[:, 0:HALF + 1:HALF, :]
                pool.tensor_tensor(both, both, both, ALU.add).then_inc(x_folded[par], 1)
                for i, (lo, hi) in enumerate(PIECES):
                    up, down, twice = t[:, lo:hi + 1, :], mirrored(t, lo, hi), doubled[:, 0:hi + 1 - lo]
                    if i > 0:
                        pool.wait_ge(x_folded[par], m * FOLDS + (i + 1))
                    pool.tensor_tensor(twice, down, down, ALU.add).then_inc(pool_steps, 1)
                    pool.tensor_tensor(up, up, down, ALU.add).then_inc(pool_steps, 1)
                    pool.wait_ge(pool_steps, steps + 2 * (i + 1))
                    pool.tensor_tensor(down, up, twice, ALU.subtract).then_inc(x_folded[par], 1)

            fold(0, 1)
            with pool.Fori(1, PAIRS) as m:
                for par in range(2):
                    pool.wait_ge(x_folded[1 - par], (m + par) * FOLDS)
                    fold(m, par)

        @block.scalar
        def _(act):
            with act.Fori(0, PAIRS) as m:
                for par in range(2):
                    n = m * 2 + par
                    for g in range(NA):
                        act.wait_ge(a_done, n * NA + (g + 1))
                        src = bank_a(g).rearrange("p (s j) -> p j s", s=A_SLOTS)
                        lo = g * A_SLOTS
                        if lo < HALF:
                            last = act.activation(U[0:BLOCK, 0:SIZE, lo:lo + A_SLOTS], src, ACT.Copy)
                        elif lo == HALF:
                            act.activation(U[0:BLOCK, 0:SIZE, lo:lo + 1], src[:, :, 0:1], ACT.Copy)
                            last = act.activation(U[0:BLOCK, 2:SIZE + 2, lo + 1:lo + A_SLOTS], src[:, :, 1:], ACT.Copy)
                        else:
                            last = act.activation(U[0:BLOCK, 2:SIZE + 2, lo:lo + A_SLOTS], src, ACT.Copy)
                        last.then_inc(a_copied, 1)
                    act.wait_ge(w_loaded[par], (m + 1) * 64)
                    for s in range(NS + 1):
                        if s < NS:
                            k = len(STEPS[s])
                            act.wait_ge(b_done, n * NS + (s + 1))
                            act.activation(mixed[s % 2][:, 0:k], bank_b(s)[:, 0:k], ACT.Copy).then_inc(b_copied, 1)
                        if s > 0:
                            t = s - 1
                            k = len(STEPS[t])
                            act.wait_ge(c_done, n * NS + (t + 1))
                            for r in range(2):
                                act.activation(hidden[t % 2][0:BLOCK, r, 0:k], bank_c(t)[:, r, 0:k], ACT.Relu,
                                               bias=b1t[par][:, r:r + 1]).then_inc(relu_done, 1)
                        if s == FLIP_AT + 1:
                            act.wait_ge(flip_done, n + 1)
                            act.activation(U[:, 0:2, 0:BLOCK], bank_flip, ACT.Copy).then_inc(flip_copied, 1)
                    for e in range(NE):
                        act.wait_ge(e_done, n * NE + (e + 1))
                        c = (e % EQ) * E_CHANNELS
                        act.activation(sums[(e // EQ) % 2][:, c:c + E_CHANNELS],
                                       bank_e(e).rearrange("p (c h) -> p c h", h=SIZE), ACT.Copy).then_inc(e_copied, 1)

        @block.vector
        def _(dve):
            for t in hidden:
                dve.memset(t[BLOCK:BLOCK + 1], 1.0).then_inc(ones_set, 1)
            t = xs[0]
            dve.wait_ge(x_loaded[0], 16 * NROWS)
            for lo, hi in PIECES:
                dve.tensor_tensor(t[:, lo:hi + 1, :], t[:, lo:hi + 1, :], mirrored(t, lo, hi),
                                  ALU.add).then_inc(dve_sums, 1)
            both = t[:, 0:HALF + 1:HALF, :]
            dve.tensor_tensor(both, both, both, ALU.add).then_inc(x_folded[0], 1)
            for i, (lo, hi) in enumerate(PIECES):
                dve.wait_ge(dve_sums, i + 1)
                dve.scalar_tensor_tensor(mirrored(t, lo, hi), mirrored(t, lo, hi), -2.0, t[:, lo:hi + 1, :],
                                         op0=ALU.mult, op1=ALU.add).then_inc(x_folded[0], 1)

            with dve.Fori(0, PAIRS) as m:
                for par in range(2):
                    n = m * 2 + par
                    t = xs[par]
                    dve.memset(U[0:BLOCK, SIZE:SIZE + 2, 0:HALF + 1], 0.0).then_inc(u_zeroed, 1)
                    dve.memset(U[0:BLOCK, 0:2, HALF + 1:SIZE], 0.0).then_inc(u_zeroed, 1)
                    dve.wait_ge(w_loaded[par], (m + 1) * 64)
                    for w in (w1t[par], w2t[par]):
                        dve.tensor_scalar(w[0:BLOCK, 0:BLOCK], w[0:BLOCK, 2 * BLOCK:], -1.0, None,
                                          ALU.mult).then_inc(w_negated, 1)
                    for s, kws in enumerate(STEPS):
                        rows = 2 * len(kws)
                        sums_d = bank_d(s).rearrange("p k (r c) -> p (k r) c", r=2)[:, 0:rows]
                        dve.wait_ge(d_done, n * NS + (s + 1))
                        dve.tensor_scalar(clipped[s % 2][:, 0:rows], sums_d, LAMBDA, -LAMBDA,
                                          ALU.min, ALU.max).then_inc(clip_done, 1)
                        dve.wait_ge(clip_done, n * NS + (s + 1))
                        dst = real_kw[:, :, :] if s == 0 else U[:, 2 * kws[0]:2 * kws[0] + rows, 0:BLOCK]
                        dve.tensor_tensor(dst, sums_d, clipped[s % 2][:, 0:rows],
                                          ALU.subtract).then_inc(shrunk, 1)
                    for q in range(NQ):
                        for j in range(FQ):
                            dve.wait_ge(f_done, n * NF + (q * FQ + j + 1))
                            c = q * CHUNK + (j % (FQ // 2)) * F_CHANNELS
                            slots = slice(0, HALF + 1) if j < FQ // 2 else slice(HALF + 1, SIZE)
                            part = t[:, slots, c:c + F_CHANNELS]
                            dve.scalar_tensor_tensor(part, part, 0.5, bank_f(j).rearrange("p c h -> p h c"),
                                                     op0=ALU.mult, op1=ALU.add).then_inc(f_added, 1)
                    dve.wait_ge(f_added, n * NF + NF)
                    for lo, hi in PIECES:
                        dve.tensor_tensor(t[:, lo:hi + 1, :], t[:, lo:hi + 1, :], mirrored(t, lo, hi),
                                          ALU.add).then_inc(unfold_even, 1)
                    for i, (lo, hi) in enumerate(PIECES):
                        dve.wait_ge(unfold_even, n * len(PIECES) + (i + 1))
                        dve.scalar_tensor_tensor(mirrored(t, lo, hi), mirrored(t, lo, hi), -2.0, t[:, lo:hi + 1, :],
                                                 op0=ALU.mult, op1=ALU.add).then_inc(unfolded, 1)

        @block.tensor
        def _(pe):
            def mat(columns):
                return mats[:, columns]

            def stage_a(m, par, n):
                pe.wait_ge(x_folded[par], (m + 1) * FOLDS)
                for g in range(NA):
                    if g >= 4:
                        pe.wait_ge(a_copied, n * NA + (g - 3))
                    for i in range(A_SLOTS):
                        slot = g * A_SLOTS + i
                        last = pe.matmul(bank_a(g)[:, i * SIZE:(i + 1) * SIZE], xs[par][:, slot, :],
                                         mat(FW_EVEN if slot <= HALF else FW_ODD), start=True, stop=True)
                    last.then_inc(a_done, 1)

            def stage_b(par, n, s):
                if s == 0:
                    pe.wait_ge(w_negated, n * 2 + 2)
                    pe.wait_ge(u_zeroed, n * 2 + 2)
                    pe.wait_ge(a_copied, n * NA + NA)
                    pe.wait_ge(f_added, n * NF)
                if s >= 2:
                    pe.wait_ge(b_copied, n * NS + (s - 1))
                for k, kw in enumerate(STEPS[s]):
                    re, im = (kw // HALF, SIZE + kw // HALF) if kw % HALF == 0 else (2 * kw, 2 * kw + 1)
                    pe.matmul(bank_b(s)[:, k], U[0:BLOCK, re], w1t[par][:, BLOCK:], start=True, stop=False)
                    last = pe.matmul(bank_b(s)[:, k], U[0:BLOCK, im], w1t[par][:, :2 * BLOCK], start=False, stop=True)
                last.then_inc(b_done, 1)

            def stage_c(n, s):
                pe.wait_ge(b_copied, n * NS + (s + 1))
                if s >= 2:
                    pe.wait_ge(relu_done, n * (2 * NS) + 2 * (s - 1))
                for k in range(len(STEPS[s])):
                    for r in range(2):
                        last = pe.matmul(bank_c(s)[:, r, k], mixed[s % 2][:, k, r * BLOCK:(r + 1) * BLOCK], mat(FH),
                                         start=True, stop=True)
                last.then_inc(c_done, 1)

            def stage_d(par, n, s):
                pe.wait_ge(relu_done, n * (2 * NS) + 2 * (s + 1))
                if s >= 2:
                    pe.wait_ge(shrunk, n * NS + (s - 1))
                for k in range(len(STEPS[s])):
                    pe.matmul(bank_d(s)[:, k], hidden[s % 2][:, 0, k], w2t[par][:, BLOCK:], start=True, stop=False)
                    last = pe.matmul(bank_d(s)[:, k], hidden[s % 2][0:BLOCK, 1, k], w2t[par][0:BLOCK, :2 * BLOCK],
                                     start=False, stop=True)
                last.then_inc(d_done, 1)

            def flip(n):
                pe.wait_ge(shrunk, n * NS + 1)
                pe.matmul(bank_flip, mat(FLIP_RE), real_kw[:, 0::2], start=True, stop=False)
                pe.matmul(bank_flip, mat(FLIP_IM), real_kw[:, 1::2], start=False, stop=True).then_inc(flip_done, 1)

            def stage_e(n, q):
                if q == 0:
                    pe.wait_ge(shrunk, n * NS + NS)
                    pe.wait_ge(flip_copied, n + 1)
                for e in range(q * EQ, (q + 1) * EQ):
                    if e >= 4:
                        pe.wait_ge(e_copied, n * NE + (e - 3))
                    for i in range(E_CHANNELS):
                        c = e * E_CHANNELS + i
                        last = pe.matmul(bank_e(e)[:, i * SIZE:(i + 1) * SIZE], U[:, 0:SIZE, c], mat(IH),
                                         start=True, stop=True)
                    last.then_inc(e_done, 1)

            def stage_f(n, q):
                pe.wait_ge(e_copied, n * NE + (q + 1) * EQ)
                for j in range(FQ):
                    if q > 0:
                        pe.wait_ge(f_added, n * NF + ((q - 1) * FQ + j + 1))
                    c = (j % (FQ // 2)) * F_CHANNELS
                    cosine = j < FQ // 2
                    rows = slice(0, HALF + 1) if cosine else slice(HALF + 1, SIZE)
                    pe.matmul(bank_f(j), mat(IW_COS if cosine else IW_SIN), sums[q % 2][:, c:c + F_CHANNELS, rows],
                              start=True, stop=True).then_inc(f_done, 1)

            pe.wait_ge(mats_loaded, 16)
            pe.wait_ge(ones_set, len(hidden))
            with pe.Fori(0, PAIRS) as m:
                for par in range(2):
                    n = m * 2 + par
                    stage_a(m, par, n)
                    for s in range(NS + 2):
                        if s < NS:
                            stage_b(par, n, s)
                        if 1 <= s <= NS:
                            stage_c(n, s - 1)
                        if s >= 2:
                            stage_d(par, n, s - 2)
                        if s == FLIP_AT:
                            flip(n)
                    for q in range(NQ + 1):
                        if q < NQ:
                            stage_e(n, q)
                        if q > 0:
                            stage_f(n, q - 1)


INPUTS = ["x", "L0_conv_w1", "L0_conv_b1", "L0_conv_w2", "L0_conv_b2"]


def kernel(**inputs):
    import concourse.bacc as bacc
    from concourse.bass_utils import run_bass_kernel_spmd

    nc = bacc.Bacc("TRN2", target_bir_lowering=False, num_devices=1)
    arrays = {name: np.ascontiguousarray(inputs[name]) for name in INPUTS}
    arrays["dft"] = constants()
    args = [nc.dram_tensor(name, a.shape, F32, kind="ExternalInput").ap() for name, a in arrays.items()]
    out = nc.dram_tensor("out", arrays["x"].shape, F32, kind="ExternalOutput").ap()
    fourier_mlp(nc, *args, out)
    result = run_bass_kernel_spmd(nc, [arrays], core_ids=[0])
    return result.results[0]["out"]
```

```python
from contextlib import ExitStack

import numpy as np

import concourse.bass as bass
from concourse import mybir

F32 = mybir.dt.float32
F32R = mybir.dt.float32r
ALU = mybir.AluOpType
ACT = mybir.ActivationFunctionType

IMAGES, SIZE, HIDDEN, BLOCKS = 4, 128, 768, 8
BLOCK = HIDDEN // BLOCKS
UNITS = IMAGES * BLOCKS
HALF = SIZE // 2
LAMBDA = 0.01

FW_EVEN, FW_ODD, FH, IH, FLIP_RE, FLIP_IM, IW_COS, IW_SIN = (slice(SIZE * i, SIZE * (i + 1)) for i in range(8))

STEPS = [(0, HALF)] + [(k, k + 1) for k in range(1, HALF - 1, 2)] + [(HALF - 1,)]
NS = len(STEPS)
FLIP_AT = 6

A_SLOTS = 4
NA = SIZE // A_SLOTS
CHUNK = 4
NQ = BLOCK // CHUNK
RING = 3
LAG = RING - 1
F_SLOTS = [(0, HALF + 1), (HALF + 1, SIZE)]
FQ = len(F_SLOTS)
NF = NQ * FQ
PIECES = [(1, 16), (17, 32), (33, 48), (49, HALF - 1)]
ROWS = [[(0, 17), (112, 128)], [(17, 33), (96, 112)], [(33, 49), (80, 96)], [(49, 80)]]
NP = len(PIECES)
FOLD_ROWS = 8
NFOLD = 2 * NP
NROWS = sum(map(len, ROWS))
A_ORDER = [g for i in range(NA // 2) for g in (i, NA - 1 - i)]

SEGMENTS = [(0, 0, BLOCK, 0, 0), (0, BLOCK, SIZE, 1, 0), (1, 0, HALF, 1, SIZE - BLOCK), (1, HALF, SIZE, 0, 0),
            (2, 0, BLOCK - HALF, 0, HALF), (2, BLOCK - HALF, SIZE, 1, 0)]
W2_COLUMNS = [0, 0, 2 * BLOCK, 4 * BLOCK, 6 * BLOCK, 6 * BLOCK]
NEGATED = [(BLOCK, SIZE, 0), (0, HALF, 2 * BLOCK), (BLOCK - HALF, HALF, 6 * BLOCK), (HALF, SIZE, 6 * BLOCK)]


def constants():
    k = np.arange(SIZE)
    cos = np.cos(2 * np.pi * np.outer(k, k) / SIZE)
    sin = np.sin(2 * np.pi * np.outer(k, k) / SIZE)
    kw = np.arange(1, HALF)
    even = np.zeros((SIZE, SIZE))
    even[:, 0], even[:, 1] = cos[:, 0], cos[:, HALF]
    even[:, 2::2], even[:, 3::2] = cos[:, kw], -sin[:, kw]
    odd = np.zeros((SIZE, SIZE))
    odd[:, 0:-2:2], odd[:, 1:-2:2] = sin[:, kw], cos[:, kw]
    odd[:, -2], odd[:, -1] = cos[:, 0], cos[:, HALF]
    fh = np.concatenate([cos[:HALF + 1], sin[HALF + 1:]])
    fh[[0, HALF]] /= 2
    ih = np.concatenate([cos[:, :HALF + 1], -sin[:, HALF + 1:]], axis=1)
    iw_cos, iw_sin = np.zeros((SIZE, SIZE)), np.zeros((SIZE, SIZE))
    iw_cos[0], iw_cos[1] = cos[0], cos[HALF]
    iw_sin[0], iw_sin[1] = -cos[0], -cos[HALF]
    iw_cos[2::2], iw_cos[3::2] = 2 * cos[kw], -2 * sin[kw]
    iw_sin[2::2], iw_sin[3::2] = -2 * sin[kw], -2 * cos[kw]
    flip = np.eye(SIZE)[(-k) % SIZE]
    scale = 1.0 / SIZE
    parts = [even * scale, odd * scale, fh, ih, (np.eye(SIZE) + flip) / 2, (np.eye(SIZE) - flip) / 2,
             iw_cos * scale, iw_sin * scale]
    return np.concatenate(parts, axis=1).astype(np.float32)


def fourier_mlp(nc, x, w1, b1, w2, b2, dft, out):
    with ExitStack() as ctx:
        def sb(name, shape, dtype=F32):
            return ctx.enter_context(nc.sbuf_tensor(name, shape, dtype))

        def sem(name):
            return ctx.enter_context(nc.semaphore(name))

        xs = [sb(f"x{i}", [SIZE, SIZE, BLOCK]) for i in range(2)]
        spectrum = sb("spectrum", [SIZE, (SIZE + 2) * SIZE])
        U = spectrum[:, :].rearrange("p (j s) -> p j s", s=SIZE)
        mixed = [sb(f"mixed{i}", [SIZE, 2, 2 * BLOCK]) for i in range(2)]
        hidden = [sb(f"hidden{i}", [SIZE, 3, SIZE]) for i in range(2)]
        biased = [sb(f"biased{i}", [SIZE, 4, BLOCK]) for i in range(2)]
        clipped = [sb(f"clipped{i}", [SIZE, 4, BLOCK]) for i in range(2)]
        real_kw = sb("real_kw", [SIZE, 4, BLOCK])
        sums_high, sums_low = (sb(f"sums_{x}", [SIZE, RING, SIZE, CHUNK], F32R) for x in ("high", "low"))
        doubled = sb("doubled", [SIZE, FOLD_ROWS, BLOCK])
        mats = sb("mats", [SIZE, 6 * SIZE])
        iw_high, iw_low = (sb(f"iw_{x}", [SIZE, 2, SIZE], F32R) for x in ("high", "low"))
        w1t = [sb(f"w1t{i}", [BLOCK, 3 * BLOCK]) for i in range(2)]
        w2t = [sb(f"w2t{i}", [SIZE, 8 * BLOCK]) for i in range(2)]
        b1t = [sb(f"b1t{i}", [SIZE, 3]) for i in range(2)]
        b2t = [sb(f"b2t{i}", [SIZE, 4, BLOCK]) for i in range(2)]
        psum = ctx.enter_context(nc.psum_tensor("psum", [SIZE, 8, 512], F32))

        def bank(i, p=SIZE, n=512):
            return psum[0:p, i, 0:n]

        def bank_a(g):
            return bank(4 + g % 4, BLOCK)

        def bank_b(s):
            return bank(s % 2, SIZE, 4 * BLOCK).rearrange("p (k y) -> p k y", k=2)

        def bank_c(s):
            return bank(2 + s % 2, SIZE, 3 * SIZE).rearrange("p (t y) -> p t y", t=3)

        def bank_d(s):
            return bank(4 + s % 2, SIZE, 4 * BLOCK)

        bank_flip = bank(6, SIZE, 2 * BLOCK).rearrange("p (k c) -> p k c", k=2)

        def bank_e(q):
            return bank(4 + q % 4).rearrange("p (c h) -> p h c", h=SIZE)

        def bank_f(q, j):
            lo, hi = F_SLOTS[j]
            return bank(FQ * (q % 2) + j, SIZE, (hi - lo) * CHUNK).rearrange("p (h c) -> p h c", c=CHUNK)

        x_loaded = [[sem(f"x_loaded{i}_{p}") for p in range(NP)] for i in range(2)]
        x_folded = [sem(f"x_folded{i}") for i in range(2)]
        x_stored = [sem(f"x_stored{i}") for i in range(2)]
        w_loaded = [sem(f"w_loaded{i}") for i in range(2)]
        W_LOADS = 1 + 3 * len(SEGMENTS) + 2
        mats_loaded, iw_loaded = sem("mats_loaded"), sem("iw_loaded")
        iw_split = sem("iw_split")
        padding_set = sem("padding_set")
        w_negated = sem("w_negated")
        u_zeroed = sem("u_zeroed")
        a_done, a_copied = sem("a_done"), sem("a_copied")
        b_done, b_copied = sem("b_done"), sem("b_copied")
        c_done, relu_done = sem("c_done"), sem("relu_done")
        d_done, bias_added, clip_done, shrunk = sem("d_done"), sem("bias_added"), sem("clip_done"), sem("shrunk")
        flip_done, flip_copied = sem("flip_done"), sem("flip_copied")
        e_done, high_copied, low_copied = sem("e_done"), sem("high_copied"), sem("low_copied")
        f_done, f_added = sem("f_done"), sem("f_added")
        pool_steps, dve_sums = sem("pool_steps"), sem("dve_sums")
        unfold_even, unfolded = sem("unfold_even"), sem("unfolded")

        block = ctx.enter_context(nc.Block())

        PAIRS = UNITS // 2
        PER_IMAGE = BLOCKS // 2

        def channels(m, par):
            return bass.ds((m % PER_IMAGE) * (2 * BLOCK) + par * BLOCK, BLOCK)

        def pixels(t, m, par):
            return t[m // PER_IMAGE].rearrange("h w c -> w h c")[:, :, channels(m, par)]

        def mirrored(t, lo, hi):
            return t[:, SIZE - hi:SIZE - lo + 1, :][:, ::-1, :]

        def tiles(s):
            return 3 if len(STEPS[s]) == 2 else 2

        @block.sync
        def _(sp):
            def load_x(m, par):
                src = pixels(x, m, par)
                for p, rows in enumerate(ROWS):
                    for lo, hi in rows:
                        sp.dma_start(xs[par][:, lo:hi, :], src[:, lo:hi, :]).then_inc(x_loaded[par][p], 16)

            def load_w(m, par):
                blk = (m % PER_IMAGE) * 2 + par

                def put(dst, src):
                    sp.dma_start(dst, src).then_inc(w_loaded[par], 16)

                put(w1t[par][:, BLOCK:].rearrange("p (r o) -> p r o", r=2), w1[:, blk].rearrange("r i o -> i r o"))
                for (tile, lo, hi, r, c), col in zip(SEGMENTS, W2_COLUMNS):
                    rows = slice(c, c + hi - lo)
                    for half in range(2):
                        put(w2t[par][lo:hi, col + half * BLOCK:col + (half + 1) * BLOCK], w2[half ^ r, blk, rows])
                    with nc.allow_non_contiguous_dma(reason="a bias on each partition"):
                        put(b1t[par][lo:hi, tile:tile + 1], b1[r, blk, rows].unsqueeze(1))
                for k in range(2):
                    put(b2t[par][:, 2 * k:2 * k + 2], b2[:, blk].partition_broadcast(SIZE))

            def store(m, par):
                dst = pixels(out, m, par)
                for i, rows in enumerate(ROWS):
                    sp.wait_ge(unfolded, (m * 2 + par) * NP + (i + 1))
                    for lo, hi in rows:
                        sp.dma_start(dst[:, lo:hi, :], xs[par][:, lo:hi, :]).then_inc(x_stored[par], 16)

            sp.dma_start(mats[:, :], dft[:, 0:6 * SIZE]).then_inc(mats_loaded, 16)
            sp.dma_start(biased[0][:, :, :].rearrange("p a b -> p (a b)")[:, 0:2 * SIZE],
                         dft[:, 6 * SIZE:]).then_inc(iw_loaded, 16)
            load_x(0, 0)
            load_w(0, 0)
            load_x(0, 1)
            load_w(0, 1)
            with sp.Fori(0, PAIRS - 1) as m:
                for par in range(2):
                    store(m, par)
                    sp.wait_ge(x_stored[par], (m + 1) * (16 * NROWS))
                    load_x(m + 1, par)
                    load_w(m + 1, par)
            for par in range(2):
                store(PAIRS - 1, par)
            for par in range(2):
                sp.wait_ge(x_stored[par], PAIRS * 16 * NROWS)

        @block.gpsimd
        def _(pool):
            def fold(m, par):
                t = xs[par]
                steps = (m * 2 + par - 1) * (2 * NFOLD)
                for i in range(NFOLD):
                    lo, hi = i * FOLD_ROWS + 1, min((i + 1) * FOLD_ROWS, HALF - 1)
                    if i % 2 == 0:
                        pool.wait_ge(x_loaded[par][i // 2], (m + 1) * (16 * len(ROWS[i // 2])))
                    up, down, twice = t[:, lo:hi + 1, :], mirrored(t, lo, hi), doubled[:, 0:hi + 1 - lo]
                    if i > 0:
                        pool.wait_ge(x_folded[par], m * NFOLD + i)
                    pool.tensor_tensor(twice, down, down, ALU.add).then_inc(pool_steps, 1)
                    pool.tensor_tensor(up, up, down, ALU.add).then_inc(pool_steps, 1)
                    ends = t[:, 0:1] if i == 0 else t[:, HALF:HALF + 1]
                    if i in (0, NFOLD - 1):
                        pool.tensor_tensor(ends, ends, ends, ALU.add)
                    pool.wait_ge(pool_steps, steps + 2 * (i + 1))
                    pool.tensor_tensor(down, up, twice, ALU.subtract).then_inc(x_folded[par], 1)

            fold(0, 1)
            with pool.Fori(1, PAIRS) as m:
                for par in range(2):
                    pool.wait_ge(x_folded[1 - par], (m + par) * NFOLD)
                    fold(m, par)

        @block.scalar
        def _(act):
            with act.Fori(0, PAIRS) as m:
                for par in range(2):
                    n = m * 2 + par
                    for i, g in enumerate(A_ORDER):
                        act.wait_ge(a_done, n * NA + (i + 1))
                        src = bank_a(i).rearrange("p (s j) -> p j s", s=A_SLOTS)
                        lo = g * A_SLOTS
                        if lo < HALF:
                            last = act.activation(U[0:BLOCK, 0:SIZE, lo:lo + A_SLOTS], src, ACT.Copy)
                        elif lo == HALF:
                            act.activation(U[0:BLOCK, 0:SIZE, lo:lo + 1], src[:, :, 0:1], ACT.Copy)
                            last = act.activation(U[0:BLOCK, 2:SIZE + 2, lo + 1:lo + A_SLOTS], src[:, :, 1:], ACT.Copy)
                        else:
                            last = act.activation(U[0:BLOCK, 2:SIZE + 2, lo:lo + A_SLOTS], src, ACT.Copy)
                        last.then_inc(a_copied, 1)
                    act.wait_ge(w_loaded[par], (m + 1) * W_LOADS * 16)
                    for s in range(NS + 1):
                        if s < NS:
                            k = len(STEPS[s])
                            act.wait_ge(b_done, n * NS + (s + 1))
                            act.activation(mixed[s % 2][:, 0:k], bank_b(s)[:, 0:k], ACT.Copy).then_inc(b_copied, 1)
                        if s > 0:
                            t = s - 1
                            act.wait_ge(c_done, n * NS + (t + 1))
                            for tile in range(tiles(t)):
                                last = act.activation(hidden[t % 2][:, tile], bank_c(t)[:, tile], ACT.Relu,
                                                      bias=b1t[par][:, tile:tile + 1])
                            last.then_inc(relu_done, 1)
                        if s == FLIP_AT + 1:
                            act.wait_ge(flip_done, n + 1)
                            act.activation(U[:, 0:2, 0:BLOCK], bank_flip, ACT.Copy).then_inc(flip_copied, 1)
                    for q in range(NQ):
                        act.wait_ge(e_done, n * NQ + (q + 1))
                        act.activation(sums_high[:, q % RING], bank_e(q), ACT.Copy).then_inc(high_copied, 1)

        @block.vector
        def _(dve):
            for t in w2t:
                dve.memset(t[HALF:SIZE, 2 * BLOCK:4 * BLOCK], 0.0).then_inc(padding_set, 1)
                dve.memset(t[0:HALF, 4 * BLOCK:6 * BLOCK], 0.0).then_inc(padding_set, 1)
            iw = biased[0][:, :, :].rearrange("p a b -> p (a b)")[:, 0:2 * SIZE].rearrange("p (a b) -> p a b", a=2)
            dve.wait_ge(iw_loaded, 16)
            dve.tensor_copy(iw_high[:, :, :], iw).then_inc(iw_split, 1)
            dve.wait_ge(iw_split, 1)
            dve.tensor_tensor(iw_low[:, :, :], iw, iw_high[:, :, :], ALU.subtract).then_inc(iw_split, 1)
            t = xs[0]
            for i, (lo, hi) in enumerate(PIECES):
                up, down = t[:, lo:hi + 1, :], mirrored(t, lo, hi)
                dve.wait_ge(x_loaded[0][i], 16 * len(ROWS[i]))
                dve.tensor_tensor(up, up, down, ALU.add).then_inc(dve_sums, 1)
                ends = t[:, 0:1] if i == 0 else t[:, HALF:HALF + 1]
                if i in (0, NP - 1):
                    dve.tensor_tensor(ends, ends, ends, ALU.add)
                dve.wait_ge(dve_sums, i + 1)
                dve.scalar_tensor_tensor(down, down, -2.0, up, op0=ALU.mult, op1=ALU.add).then_inc(x_folded[0], 2)

            with dve.Fori(0, PAIRS) as m:
                for par in range(2):
                    n = m * 2 + par
                    t = xs[par]
                    dve.memset(U[0:BLOCK, SIZE:SIZE + 2, 0:HALF + 1], 0.0).then_inc(u_zeroed, 1)
                    dve.memset(U[0:BLOCK, 0:2, HALF + 1:SIZE], 0.0).then_inc(u_zeroed, 1)
                    dve.wait_ge(w_loaded[par], (m + 1) * W_LOADS * 16)
                    w1_im = slice(0, BLOCK)
                    dve.tensor_scalar(w1t[par][:, w1_im], w1t[par][:, 2 * BLOCK:], -1.0, None,
                                      ALU.mult).then_inc(w_negated, 1)
                    for lo, hi, col in NEGATED:
                        part = w2t[par][lo:hi, col:col + BLOCK]
                        dve.tensor_scalar(part, part, -1.0, None, ALU.mult).then_inc(w_negated, 1)
                    for s, kws in enumerate(STEPS):
                        rows = 2 * len(kws)
                        v, c = biased[s % 2][:, 0:rows], clipped[s % 2][:, 0:rows]
                        dve.wait_ge(d_done, n * NS + (s + 1))
                        dve.tensor_tensor(v, bank_d(s).rearrange("p (k c) -> p k c", c=BLOCK)[:, 0:rows],
                                          b2t[par][:, 0:rows], ALU.add).then_inc(bias_added, 1)
                        dve.wait_ge(bias_added, n * NS + (s + 1))
                        dve.tensor_scalar(c, v, LAMBDA, -LAMBDA, ALU.min, ALU.max).then_inc(clip_done, 1)
                        dve.wait_ge(clip_done, n * NS + (s + 1))
                        dst = real_kw[:, :, :] if s == 0 else U[:, 2 * kws[0]:2 * kws[0] + rows, 0:BLOCK]
                        dve.tensor_tensor(dst, v, c, ALU.subtract).then_inc(shrunk, 1)
                    for q in range(NQ + LAG):
                        if q < NQ:
                            dve.wait_ge(high_copied, n * NQ + (q + 1))
                            dve.tensor_tensor(sums_low[:, q % RING], bank_e(q), sums_high[:, q % RING],
                                              ALU.subtract).then_inc(low_copied, 1)
                        if q >= LAG:
                            c = (q - LAG) * CHUNK
                            for j, (lo, hi) in enumerate(F_SLOTS):
                                dve.wait_ge(f_done, n * NF + ((q - LAG) * FQ + (j + 1)))
                                part = t[:, lo:hi, c:c + CHUNK]
                                dve.scalar_tensor_tensor(part, part, 0.5, bank_f(q - LAG, j), op0=ALU.mult,
                                                         op1=ALU.add).then_inc(f_added, 1)
                    dve.wait_ge(f_added, n * NF + NF)
                    for lo, hi in PIECES:
                        dve.tensor_tensor(t[:, lo:hi + 1, :], t[:, lo:hi + 1, :], mirrored(t, lo, hi),
                                          ALU.add).then_inc(unfold_even, 1)
                    for i, (lo, hi) in enumerate(PIECES):
                        dve.wait_ge(unfold_even, n * NP + (i + 1))
                        dve.scalar_tensor_tensor(mirrored(t, lo, hi), mirrored(t, lo, hi), -2.0, t[:, lo:hi + 1, :],
                                                 op0=ALU.mult, op1=ALU.add).then_inc(unfolded, 1)

        @block.tensor
        def _(pe):
            def mat(columns):
                return mats[:, columns]

            def stage_a(m, par, n):
                for at, g in enumerate(A_ORDER):
                    if at % (NA // NP) == 0:
                        pe.wait_ge(x_folded[par], m * NFOLD + 2 * (at // (NA // NP) + 1))
                    if at >= 4:
                        pe.wait_ge(a_copied, n * NA + (at - 3))
                    for i in range(A_SLOTS):
                        slot = g * A_SLOTS + i
                        last = pe.matmul(bank_a(at)[:, i * SIZE:(i + 1) * SIZE], xs[par][:, slot, :],
                                         mat(FW_EVEN if slot <= HALF else FW_ODD), start=True, stop=True)
                    last.then_inc(a_done, 1)

            def stage_b(par, n, s):
                if s == 0:
                    pe.wait_ge(w_negated, (n + 1) * (1 + len(NEGATED)))
                    pe.wait_ge(u_zeroed, n * 2 + 2)
                    pe.wait_ge(a_copied, n * NA + NA)
                    pe.wait_ge(f_added, n * NF)
                if s >= 2:
                    pe.wait_ge(b_copied, n * NS + (s - 1))
                for k, kw in enumerate(STEPS[s]):
                    re, im = (kw // HALF, SIZE + kw // HALF) if kw % HALF == 0 else (2 * kw, 2 * kw + 1)
                    pe.matmul(bank_b(s)[:, k], U[0:BLOCK, re], w1t[par][:, BLOCK:], start=True, stop=False)
                    last = pe.matmul(bank_b(s)[:, k], U[0:BLOCK, im], w1t[par][:, :2 * BLOCK], start=False, stop=True)
                last.then_inc(b_done, 1)

            def stage_c(n, s):
                pe.wait_ge(b_copied, n * NS + (s + 1))
                if s >= 2:
                    pe.wait_ge(relu_done, n * NS + (s - 1))
                flat = mixed[s % 2][:, :, :].rearrange("p k y -> p (k y)")
                for tile in range(tiles(s)):
                    last = pe.matmul(bank_c(s)[:, tile], flat[:, tile * SIZE:(tile + 1) * SIZE], mat(FH),
                                     start=True, stop=True)
                last.then_inc(c_done, 1)

            def stage_d(par, n, s):
                pe.wait_ge(relu_done, n * NS + (s + 1))
                if s >= 2:
                    pe.wait_ge(bias_added, n * NS + (s - 1))
                one, both = 2 * BLOCK, len(STEPS[s]) * 2 * BLOCK
                h, w, sums_d = hidden[s % 2], w2t[par], bank_d(s)
                pe.matmul(sums_d[:, 0:both], h[:, 1], w[:, one:one + both], start=True, stop=False)
                last = pe.matmul(sums_d[:, 0:one], h[:, 0], w[:, 0:one], start=False, stop=both == one)
                if both > one:
                    last = pe.matmul(sums_d[:, one:both], h[:, 2], w[:, 3 * one:], start=False, stop=True)
                last.then_inc(d_done, 1)

            def flip(n):
                pe.wait_ge(shrunk, n * NS + 1)
                pe.matmul(bank_flip, mat(FLIP_RE), real_kw[:, 0::2], start=True, stop=False)
                pe.matmul(bank_flip, mat(FLIP_IM), real_kw[:, 1::2], start=False, stop=True).then_inc(flip_done, 1)

            def stage_e(n, q):
                if q == 0:
                    pe.wait_ge(shrunk, n * NS + NS)
                    pe.wait_ge(flip_copied, n + 1)
                if q >= 4:
                    pe.wait_ge(low_copied, n * NQ + (q - 3))
                for i in range(CHUNK):
                    last = pe.matmul(bank_e(q)[:, :, i], U[:, 0:SIZE, q * CHUNK + i], mat(IH), start=True, stop=True)
                last.then_inc(e_done, 1)

            def stage_f(n, q):
                pe.wait_ge(low_copied, n * NQ + (q + 1))
                for j, (lo, hi) in enumerate(F_SLOTS):
                    if q >= 2:
                        pe.wait_ge(f_added, n * NF + ((q - 2) * FQ + (j + 1)))
                    high, low = sums_high[:, q % RING, lo:hi], sums_low[:, q % RING, lo:hi]
                    pe.matmul(bank_f(q, j), iw_high[:, j], high, start=True, stop=False)
                    pe.matmul(bank_f(q, j), iw_high[:, j], low, start=False, stop=False)
                    pe.matmul(bank_f(q, j), iw_low[:, j], high, start=False, stop=True).then_inc(f_done, 1)

            pe.wait_ge(iw_split, 2)
            pe.wait_ge(mats_loaded, 16)
            pe.wait_ge(padding_set, 2 * len(w2t))
            with pe.Fori(0, PAIRS) as m:
                for par in range(2):
                    n = m * 2 + par
                    stage_a(m, par, n)
                    for s in range(NS + 2):
                        if s < NS:
                            stage_b(par, n, s)
                        if 1 <= s <= NS:
                            stage_c(n, s - 1)
                        if s >= 2:
                            stage_d(par, n, s - 2)
                        if s == FLIP_AT:
                            flip(n)
                    for q in range(NQ + LAG):
                        if q < NQ:
                            stage_e(n, q)
                        if q >= LAG:
                            stage_f(n, q - LAG)


INPUTS = ["x", "L0_conv_w1", "L0_conv_b1", "L0_conv_w2", "L0_conv_b2"]


def kernel(**inputs):
    import concourse.bacc as bacc
    from concourse.bass_utils import run_bass_kernel_spmd

    nc = bacc.Bacc("TRN2", target_bir_lowering=False, num_devices=1)
    arrays = {name: np.ascontiguousarray(inputs[name]) for name in INPUTS}
    arrays["dft"] = constants()
    args = [nc.dram_tensor(name, a.shape, F32, kind="ExternalInput").ap() for name, a in arrays.items()]
    out = nc.dram_tensor("out", arrays["x"].shape, F32, kind="ExternalOutput").ap()
    fourier_mlp(nc, *args, out)
    result = run_bass_kernel_spmd(nc, [arrays], core_ids=[0])
    return result.results[0]["out"]
```

```python
from contextlib import ExitStack

import numpy as np

import concourse.bass as bass
from concourse import mybir

F32 = mybir.dt.float32
F32R = mybir.dt.float32r
ALU = mybir.AluOpType
ACT = mybir.ActivationFunctionType

IMAGES, SIZE, HIDDEN, BLOCKS = 4, 128, 768, 8
BLOCK = HIDDEN // BLOCKS
UNITS = IMAGES * BLOCKS
HALF = SIZE // 2
LAMBDA = 0.01

FW_EVEN, FW_ODD, FH, IH, FLIP_RE, FLIP_IM, IW_COS, IW_SIN = (slice(SIZE * i, SIZE * (i + 1)) for i in range(8))

STEPS = [(0, HALF)] + [(k, k + 1) for k in range(1, HALF - 1, 2)] + [(HALF - 1,)]
NS = len(STEPS)

A_SLOTS = 4
NA = SIZE // A_SLOTS
CHUNK = 4
NQ = BLOCK // CHUNK
RING = 3
LAG = RING - 1
F_SLOTS = [(0, HALF + 1), (HALF + 1, SIZE)]
FQ = len(F_SLOTS)
NF = NQ * FQ
PIECES = [(1, 16), (17, 32), (33, 48), (49, HALF - 1)]
ROWS = [[(0, 17), (112, 128)], [(17, 33), (96, 112)], [(33, 49), (80, 96)], [(49, 80)]]
NP = len(PIECES)
FOLD_ROWS = 8
NFOLD = 2 * NP
NROWS = sum(map(len, ROWS))
A_ORDER = [g for i in range(NA // 2) for g in (i, NA - 1 - i)]

SEGMENTS = [(0, 0, BLOCK, 0, 0), (0, BLOCK, SIZE, 1, 0), (1, 0, HALF, 1, SIZE - BLOCK), (1, HALF, SIZE, 0, 0),
            (2, 0, BLOCK - HALF, 0, HALF), (2, BLOCK - HALF, SIZE, 1, 0)]
W2_COLUMNS = [tile * 2 * BLOCK for tile, *_ in SEGMENTS]
NEGATED = [(BLOCK, SIZE, 0), (0, HALF, 2 * BLOCK), (BLOCK - HALF, HALF, 4 * BLOCK), (HALF, SIZE, 4 * BLOCK)]


def constants():
    k = np.arange(SIZE)
    cos = np.cos(2 * np.pi * np.outer(k, k) / SIZE)
    sin = np.sin(2 * np.pi * np.outer(k, k) / SIZE)
    kw = np.arange(1, HALF)
    even = np.zeros((SIZE, SIZE))
    even[:, 0], even[:, 1] = cos[:, 0], cos[:, HALF]
    even[:, 2::2], even[:, 3::2] = cos[:, kw], -sin[:, kw]
    odd = np.zeros((SIZE, SIZE))
    odd[:, 0:-2:2], odd[:, 1:-2:2] = sin[:, kw], cos[:, kw]
    odd[:, -2], odd[:, -1] = cos[:, 0], cos[:, HALF]
    fh = np.concatenate([cos[:HALF + 1], sin[HALF + 1:]])
    fh[[0, HALF]] /= 2
    ih = np.concatenate([cos[:, :HALF + 1], -sin[:, HALF + 1:]], axis=1)
    iw_cos, iw_sin = np.zeros((SIZE, SIZE)), np.zeros((SIZE, SIZE))
    iw_cos[0], iw_cos[1] = cos[0], cos[HALF]
    iw_sin[0], iw_sin[1] = -cos[0], -cos[HALF]
    iw_cos[2::2], iw_cos[3::2] = 2 * cos[kw], -2 * sin[kw]
    iw_sin[2::2], iw_sin[3::2] = -2 * sin[kw], -2 * cos[kw]
    flip = np.eye(SIZE)[(-k) % SIZE]
    scale = 1.0 / SIZE
    parts = [even * scale, odd * scale, fh, ih, (np.eye(SIZE) + flip) / 2, (np.eye(SIZE) - flip) / 2,
             iw_cos * scale, iw_sin * scale]
    return np.concatenate(parts, axis=1).astype(np.float32)


def fourier_mlp(nc, x, w1, b1, w2, b2, dft, out):
    with ExitStack() as ctx:
        def sb(name, shape, dtype=F32):
            return ctx.enter_context(nc.sbuf_tensor(name, shape, dtype))

        def sem(name):
            return ctx.enter_context(nc.semaphore(name))

        xs = [sb(f"x{i}", [SIZE, SIZE, BLOCK]) for i in range(2)]
        spectrum = sb("spectrum", [SIZE, (SIZE + 2) * SIZE])
        U = spectrum[:, :].rearrange("p (j s) -> p j s", s=SIZE)
        mixed = [sb(f"mixed{i}", [SIZE, 2, 2 * BLOCK]) for i in range(2)]
        hidden = [sb(f"hidden{i}", [SIZE, 2, SIZE]) for i in range(2)]
        hidden_high, hidden_low = ([sb(f"hidden_{x}{i}", [SIZE, SIZE], F32R) for i in range(2)] for x in ("high", "low"))
        relu1 = [sb(f"relu1_{i}", [SIZE, SIZE]) for i in range(2)]
        biased = [sb(f"biased{i}", [SIZE, 4, BLOCK]) for i in range(2)]
        clipped = [sb(f"clipped{i}", [SIZE, 4, BLOCK]) for i in range(2)]
        real_kw = sb("real_kw", [SIZE, 4, BLOCK])
        sums_high, sums_low = (sb(f"sums_{x}", [SIZE, RING, SIZE, CHUNK], F32R) for x in ("high", "low"))
        doubled = sb("doubled", [SIZE, FOLD_ROWS, BLOCK])
        mats = sb("mats", [SIZE, 6 * SIZE])
        iw_high, iw_low = (sb(f"iw_{x}", [SIZE, 2, SIZE], F32R) for x in ("high", "low"))
        w1t = [sb(f"w1t{i}", [BLOCK, 3 * BLOCK]) for i in range(2)]
        w2t = [sb(f"w2t{i}", [SIZE, 6 * BLOCK]) for i in range(2)]
        w2_high, w2_low = (sb(f"w2_{x}", [SIZE, 4 * BLOCK], F32R) for x in ("high", "low"))
        b1t = [sb(f"b1t{i}", [SIZE, 3]) for i in range(2)]
        b2t = [sb(f"b2t{i}", [SIZE, 2, BLOCK]) for i in range(2)]
        psum = ctx.enter_context(nc.psum_tensor("psum", [SIZE, 8, 512], F32))

        def bank(i, p=SIZE, n=512):
            return psum[0:p, i, 0:n]

        E_BANKS, F_BANKS = 3, [0, 1, 7]
        F_LAST = {NF - 3: 4, NF - 2: 5, NF - 1: 0}

        AHEAD = 2

        def bank_a(at):
            return bank(2 + at if at < AHEAD else 4 + at % 4, BLOCK)

        def bank_b(s):
            return bank(s % 2, SIZE, 4 * BLOCK).rearrange("p (k y) -> p k y", k=2)

        def bank_c(s):
            outer = bank(2 + s % 2, SIZE, 2 * SIZE)
            return [outer[:, 0:SIZE], bank(6 + s % 2, SIZE, SIZE), outer[:, SIZE:]]

        def bank_d(s):
            return bank(4 + s % 2, SIZE, 4 * BLOCK)

        bank_flip = bank(6, SIZE, 2 * BLOCK).rearrange("p (k c) -> p k c", k=2)

        def bank_e(q):
            return bank(4 + q % E_BANKS).rearrange("p (c h) -> p h c", h=SIZE)

        def bank_f(q, j):
            lo, hi = F_SLOTS[j]
            k = q * FQ + j
            return bank(F_LAST.get(k, F_BANKS[k % len(F_BANKS)]), SIZE, (hi - lo) * CHUNK).rearrange("p (h c) -> p h c", c=CHUNK)

        x_loaded = [[sem(f"x_loaded{i}_{p}") for p in range(NP)] for i in range(2)]
        x_folded = [sem(f"x_folded{i}") for i in range(2)]
        x_stored = [sem(f"x_stored{i}") for i in range(2)]
        w_loaded = [sem(f"w_loaded{i}") for i in range(2)]
        W_LOADS = 1 + 3 * len(SEGMENTS) + 1
        mats_loaded, iw_loaded = sem("mats_loaded"), sem("iw_loaded")
        iw_split = sem("iw_split")
        padding_set = sem("padding_set")
        w_negated, w2_split = sem("w_negated"), sem("w2_split")
        high_done, relu1_done, low_done = sem("high_done"), sem("relu1_done"), sem("low_done")
        u_zeroed = sem("u_zeroed")
        a_done, a_copied = sem("a_done"), sem("a_copied")
        b_done, b_copied = sem("b_done"), sem("b_copied")
        c_done, relu_done = sem("c_done"), sem("relu_done")
        d_done, bias_added, clip_done, shrunk = sem("d_done"), sem("bias_added"), sem("clip_done"), sem("shrunk")
        flip_done, flip_copied = sem("flip_done"), sem("flip_copied")
        e_done, high_copied, low_copied = sem("e_done"), sem("high_copied"), sem("low_copied")
        f_done, f_added = sem("f_done"), sem("f_added")
        pool_steps, dve_sums = sem("pool_steps"), sem("dve_sums")
        unfold_even, unfolded = sem("unfold_even"), sem("unfolded")

        block = ctx.enter_context(nc.Block())

        PAIRS = UNITS // 2
        PER_IMAGE = BLOCKS // 2

        def channels(m, par):
            return bass.ds((m % PER_IMAGE) * (2 * BLOCK) + par * BLOCK, BLOCK)

        def pixels(t, m, par):
            return t[m // PER_IMAGE].rearrange("h w c -> w h c")[:, :, channels(m, par)]

        def mirrored(t, lo, hi):
            return t[:, SIZE - hi:SIZE - lo + 1, :][:, ::-1, :]

        def tiles(s):
            return 3 if len(STEPS[s]) == 2 else 2

        @block.sync
        def _(sp):
            def load_x(m, par):
                src = pixels(x, m, par)
                for p, rows in enumerate(ROWS):
                    for lo, hi in rows:
                        sp.dma_start(xs[par][:, lo:hi, :], src[:, lo:hi, :]).then_inc(x_loaded[par][p], 16)

            def load_w(m, par):
                blk = (m % PER_IMAGE) * 2 + par

                def put(dst, src):
                    sp.dma_start(dst, src).then_inc(w_loaded[par], 16)

                put(w1t[par][:, BLOCK:].rearrange("p (r o) -> p r o", r=2), w1[:, blk].rearrange("r i o -> i r o"))
                for (tile, lo, hi, r, c), col in zip(SEGMENTS, W2_COLUMNS):
                    rows = slice(c, c + hi - lo)
                    for half in range(2):
                        put(w2t[par][lo:hi, col + half * BLOCK:col + (half + 1) * BLOCK], w2[half ^ r, blk, rows])
                    with nc.allow_non_contiguous_dma(reason="a bias on each partition"):
                        put(b1t[par][lo:hi, tile:tile + 1], b1[r, blk, rows].unsqueeze(1))
                put(b2t[par][:, :, :], b2[:, blk].partition_broadcast(SIZE))

            def store(m, par):
                dst = pixels(out, m, par)
                for i, rows in enumerate(ROWS):
                    sp.wait_ge(unfolded, (m * 2 + par) * NP + (i + 1))
                    for lo, hi in rows:
                        sp.dma_start(dst[:, lo:hi, :], xs[par][:, lo:hi, :]).then_inc(x_stored[par], 16)

            sp.dma_start(mats[:, :], dft[:, 0:6 * SIZE]).then_inc(mats_loaded, 16)
            sp.dma_start(biased[0][:, :, :].rearrange("p a b -> p (a b)")[:, 0:2 * SIZE],
                         dft[:, 6 * SIZE:]).then_inc(iw_loaded, 16)
            load_x(0, 0)
            load_w(0, 0)
            load_x(0, 1)
            load_w(0, 1)
            with sp.Fori(0, PAIRS - 1) as m:
                for par in range(2):
                    store(m, par)
                    sp.wait_ge(x_stored[par], (m + 1) * (16 * NROWS))
                    load_x(m + 1, par)
                    load_w(m + 1, par)
            for par in range(2):
                store(PAIRS - 1, par)
            for par in range(2):
                sp.wait_ge(x_stored[par], PAIRS * 16 * NROWS)

        @block.gpsimd
        def _(pool):
            def fold(m, par):
                t = xs[par]
                steps = (m * 2 + par - 1) * (2 * NFOLD)
                for i in range(NFOLD):
                    lo, hi = i * FOLD_ROWS + 1, min((i + 1) * FOLD_ROWS, HALF - 1)
                    if i % 2 == 0:
                        pool.wait_ge(x_loaded[par][i // 2], (m + 1) * (16 * len(ROWS[i // 2])))
                    up, down, twice = t[:, lo:hi + 1, :], mirrored(t, lo, hi), doubled[:, 0:hi + 1 - lo]
                    if i > 0:
                        pool.wait_ge(x_folded[par], m * NFOLD + i)
                    pool.tensor_tensor(twice, down, down, ALU.add).then_inc(pool_steps, 1)
                    pool.tensor_tensor(up, up, down, ALU.add).then_inc(pool_steps, 1)
                    ends = t[:, 0:1] if i == 0 else t[:, HALF:HALF + 1]
                    if i in (0, NFOLD - 1):
                        pool.tensor_tensor(ends, ends, ends, ALU.add)
                    pool.wait_ge(pool_steps, steps + 2 * (i + 1))
                    pool.tensor_tensor(down, up, twice, ALU.subtract).then_inc(x_folded[par], 1)

            fold(0, 1)
            with pool.Fori(1, PAIRS) as m:
                for par in range(2):
                    pool.wait_ge(x_folded[1 - par], (m + par) * NFOLD)
                    fold(m, par)

        @block.scalar
        def _(act):
            with act.Fori(0, PAIRS) as m:
                for par in range(2):
                    n = m * 2 + par
                    for i, g in enumerate(A_ORDER):
                        act.wait_ge(a_done, n * NA + (i + 1))
                        src = bank_a(i).rearrange("p (s j) -> p j s", s=A_SLOTS)
                        lo = g * A_SLOTS
                        if lo < HALF:
                            last = act.activation(U[0:BLOCK, 0:SIZE, lo:lo + A_SLOTS], src, ACT.Copy)
                        elif lo == HALF:
                            act.activation(U[0:BLOCK, 0:SIZE, lo:lo + 1], src[:, :, 0:1], ACT.Copy)
                            last = act.activation(U[0:BLOCK, 2:SIZE + 2, lo + 1:lo + A_SLOTS], src[:, :, 1:], ACT.Copy)
                        else:
                            last = act.activation(U[0:BLOCK, 2:SIZE + 2, lo:lo + A_SLOTS], src, ACT.Copy)
                        last.then_inc(a_copied, 1)
                    act.wait_ge(w_loaded[par], (m + 1) * W_LOADS * 16)
                    for s in range(NS + 1):
                        if s < NS:
                            k = len(STEPS[s])
                            act.wait_ge(b_done, n * NS + (s + 1))
                            act.activation(mixed[s % 2][:, 0:k], bank_b(s)[:, 0:k], ACT.Copy).then_inc(b_copied, 1)
                        if s > 0:
                            t = s - 1
                            act.wait_ge(c_done, n * NS + (t + 1))
                            act.activation(hidden_high[t % 2][:, :], bank_c(t)[1], ACT.Relu,
                                           bias=b1t[par][:, 1:2]).then_inc(high_done, 1)
                            for tile in range(0, tiles(t), 2):
                                last = act.activation(hidden[t % 2][:, tile // 2], bank_c(t)[tile], ACT.Relu,
                                                      bias=b1t[par][:, tile:tile + 1])
                            last.then_inc(relu_done, 1)
                    act.wait_ge(flip_done, n + 1)
                    act.activation(U[:, 0:2, 0:BLOCK], bank_flip, ACT.Copy).then_inc(flip_copied, 1)
                    for q in range(NQ):
                        act.wait_ge(e_done, n * NQ + (q + 1))
                        act.activation(sums_high[:, q % RING], bank_e(q), ACT.Copy).then_inc(high_copied, 1)

        @block.vector
        def _(dve):
            for t in (w2_high, w2_low):
                dve.memset(t[HALF:SIZE, 0:2 * BLOCK].bitcast(F32), 0.0).then_inc(padding_set, 1)
                dve.memset(t[0:HALF, 2 * BLOCK:].bitcast(F32), 0.0).then_inc(padding_set, 1)
            iw = biased[0][:, :, :].rearrange("p a b -> p (a b)")[:, 0:2 * SIZE].rearrange("p (a b) -> p a b", a=2)
            dve.wait_ge(iw_loaded, 16)
            dve.tensor_copy(iw_high[:, :, :], iw).then_inc(iw_split, 1)
            dve.wait_ge(iw_split, 1)
            dve.tensor_tensor(iw_low[:, :, :], iw, iw_high[:, :, :], ALU.subtract).then_inc(iw_split, 1)
            t = xs[0]
            for i, (lo, hi) in enumerate(PIECES):
                up, down = t[:, lo:hi + 1, :], mirrored(t, lo, hi)
                dve.wait_ge(x_loaded[0][i], 16 * len(ROWS[i]))
                dve.tensor_tensor(up, up, down, ALU.add).then_inc(dve_sums, 1)
                ends = t[:, 0:1] if i == 0 else t[:, HALF:HALF + 1]
                if i in (0, NP - 1):
                    dve.tensor_tensor(ends, ends, ends, ALU.add)
                dve.wait_ge(dve_sums, i + 1)
                dve.scalar_tensor_tensor(down, down, -2.0, up, op0=ALU.mult, op1=ALU.add).then_inc(x_folded[0], 2)

            with dve.Fori(0, PAIRS) as m:
                for par in range(2):
                    n = m * 2 + par
                    x_unit = xs[par]
                    dve.memset(U[0:BLOCK, SIZE:SIZE + 2, 0:HALF + 1], 0.0).then_inc(u_zeroed, 1)
                    dve.memset(U[0:BLOCK, 0:2, HALF + 1:SIZE], 0.0).then_inc(u_zeroed, 1)
                    dve.wait_ge(w_loaded[par], (m + 1) * W_LOADS * 16)
                    w1_im = slice(0, BLOCK)
                    dve.tensor_scalar(w1t[par][:, w1_im], w1t[par][:, 2 * BLOCK:], -1.0, None,
                                      ALU.mult).then_inc(w_negated, 1)
                    for lo, hi, col in NEGATED:
                        part = w2t[par][lo:hi, col:col + BLOCK]
                        dve.tensor_scalar(part, part, -1.0, None, ALU.mult).then_inc(w_negated, 1)
                    dve.wait_ge(w_negated, (n + 1) * (1 + len(NEGATED)))
                    halves = [(slice(0, HALF), slice(0, 2 * BLOCK)), (slice(HALF, SIZE), slice(2 * BLOCK, 4 * BLOCK))]
                    for rows, cols in halves:
                        dve.tensor_copy(w2_high[rows, cols], w2t[par][rows, 2 * BLOCK:4 * BLOCK]).then_inc(w2_split, 1)
                    dve.wait_ge(w2_split, n * 4 + 2)
                    for rows, cols in halves:
                        dve.tensor_tensor(w2_low[rows, cols], w2t[par][rows, 2 * BLOCK:4 * BLOCK], w2_high[rows, cols],
                                          ALU.subtract).then_inc(w2_split, 1)
                    for s in range(NS + 1):
                        if s < NS:
                            dve.wait_ge(high_done, n * NS + (s + 1))
                            dve.tensor_scalar(relu1[s % 2][:, :], bank_c(s)[1], b1t[par][:, 1:2], 0.0,
                                              ALU.add, ALU.max).then_inc(relu1_done, 1)
                            dve.wait_ge(relu1_done, n * NS + (s + 1))
                            dve.tensor_tensor(hidden_low[s % 2][:, :], relu1[s % 2][:, :], hidden_high[s % 2][:, :],
                                              ALU.subtract).then_inc(low_done, 1)
                        if s > 0:
                            t, kws = s - 1, STEPS[s - 1]
                            rows = 2 * len(kws)
                            v, c = biased[t % 2][:, 0:rows], clipped[t % 2][:, 0:rows]
                            pairs = "p (k r) c -> p k r c"
                            dve.wait_ge(d_done, n * NS + (t + 1))
                            dve.tensor_tensor(
                                v.rearrange(pairs, r=2),
                                bank_d(t).rearrange("p (k r c) -> p k r c", r=2, c=BLOCK)[:, 0:len(kws)],
                                b2t[par][:, :, :].unsqueeze(1).broadcast_to([SIZE, len(kws), 2, BLOCK]),
                                ALU.add).then_inc(bias_added, 1)
                            dve.wait_ge(bias_added, n * NS + (t + 1))
                            dve.tensor_scalar(c, v, LAMBDA, -LAMBDA, ALU.min, ALU.max).then_inc(clip_done, 1)
                            dve.wait_ge(clip_done, n * NS + (t + 1))
                            dst = real_kw[:, :, :] if t == 0 else U[:, 2 * kws[0]:2 * kws[0] + rows, 0:BLOCK]
                            dve.tensor_tensor(dst, v, c, ALU.subtract).then_inc(shrunk, 1)
                    for q in range(NQ + LAG):
                        if q < NQ:
                            dve.wait_ge(high_copied, n * NQ + (q + 1))
                            dve.tensor_tensor(sums_low[:, q % RING], bank_e(q), sums_high[:, q % RING],
                                              ALU.subtract).then_inc(low_copied, 1)
                        if q >= LAG:
                            c = (q - LAG) * CHUNK
                            for j, (lo, hi) in enumerate(F_SLOTS):
                                dve.wait_ge(f_done, n * NF + ((q - LAG) * FQ + (j + 1)))
                                part = x_unit[:, lo:hi, c:c + CHUNK]
                                dve.scalar_tensor_tensor(part, part, 0.5, bank_f(q - LAG, j), op0=ALU.mult,
                                                         op1=ALU.add).then_inc(f_added, 1)
                    dve.wait_ge(f_added, n * NF + NF)
                    for i in range(NP + 1):
                        if i < NP:
                            lo, hi = PIECES[i]
                            dve.tensor_tensor(x_unit[:, lo:hi + 1, :], x_unit[:, lo:hi + 1, :], mirrored(x_unit, lo, hi),
                                              ALU.add).then_inc(unfold_even, 1)
                        if i > 0:
                            lo, hi = PIECES[i - 1]
                            dve.wait_ge(unfold_even, n * NP + i)
                            dve.scalar_tensor_tensor(mirrored(x_unit, lo, hi), mirrored(x_unit, lo, hi), -2.0,
                                                     x_unit[:, lo:hi + 1, :], op0=ALU.mult,
                                                     op1=ALU.add).then_inc(unfolded, 1)

        @block.tensor
        def _(pe):
            def mat(columns):
                return mats[:, columns]

            def stage_a(m, par, n, first, end):
                for at, g in list(enumerate(A_ORDER))[first:end]:
                    if at % (NA // NP) == 0:
                        pe.wait_ge(x_folded[par], m * NFOLD + 2 * (at // (NA // NP) + 1))
                    if at >= AHEAD + 4:
                        pe.wait_ge(a_copied, n * NA + (at - 3))
                    if at == 3:
                        pe.wait_ge(f_added, n * NF)
                    for i in range(A_SLOTS):
                        slot = g * A_SLOTS + i
                        last = pe.matmul(bank_a(at)[:, i * SIZE:(i + 1) * SIZE], xs[par][:, slot, :],
                                         mat(FW_EVEN if slot <= HALF else FW_ODD), start=True, stop=True)
                    last.then_inc(a_done, 1)

            def stage_b(par, n, s):
                if s == 0:
                    pe.wait_ge(w_negated, (n + 1) * (1 + len(NEGATED)))
                    pe.wait_ge(u_zeroed, n * 2 + 2)
                    pe.wait_ge(a_copied, n * NA + NA)
                    pe.wait_ge(f_added, n * NF)
                if s >= 2:
                    pe.wait_ge(b_copied, n * NS + (s - 1))
                for k, kw in enumerate(STEPS[s]):
                    re, im = (kw // HALF, SIZE + kw // HALF) if kw % HALF == 0 else (2 * kw, 2 * kw + 1)
                    pe.matmul(bank_b(s)[:, k], U[0:BLOCK, re], w1t[par][:, BLOCK:], start=True, stop=False)
                    last = pe.matmul(bank_b(s)[:, k], U[0:BLOCK, im], w1t[par][:, :2 * BLOCK], start=False, stop=True)
                last.then_inc(b_done, 1)

            def stage_c(n, s):
                pe.wait_ge(b_copied, n * NS + (s + 1))
                if s >= 2:
                    pe.wait_ge(relu_done, n * NS + (s - 1))
                    pe.wait_ge(relu1_done, n * NS + (s - 1))
                flat = mixed[s % 2][:, :, :].rearrange("p k y -> p (k y)")
                for tile in range(tiles(s)):
                    last = pe.matmul(bank_c(s)[tile], flat[:, tile * SIZE:(tile + 1) * SIZE], mat(FH),
                                     start=True, stop=True)
                last.then_inc(c_done, 1)

            def stage_d(par, n, s):
                if s == 0:
                    pe.wait_ge(w2_split, n * 4 + 4)
                pe.wait_ge(relu_done, n * NS + (s + 1))
                pe.wait_ge(low_done, n * NS + (s + 1))
                if s >= 2:
                    pe.wait_ge(bias_added, n * NS + (s - 1))
                one, both = 2 * BLOCK, len(STEPS[s]) * 2 * BLOCK
                h, high, low, w, sums_d = hidden[s % 2], hidden_high[s % 2], hidden_low[s % 2], w2t[par], bank_d(s)
                pe.matmul(sums_d[:, 0:both], high[:, :], w2_high[:, 0:both], start=True, stop=False)
                pe.matmul(sums_d[:, 0:both], low[:, :], w2_high[:, 0:both], start=False, stop=False)
                pe.matmul(sums_d[:, 0:both], high[:, :], w2_low[:, 0:both], start=False, stop=False)
                last = pe.matmul(sums_d[:, 0:one], h[:, 0], w[:, 0:one], start=False, stop=both == one)
                if both > one:
                    last = pe.matmul(sums_d[:, one:both], h[:, 1], w[:, 2 * one:], start=False, stop=True)
                last.then_inc(d_done, 1)

            def flip(n):
                pe.wait_ge(shrunk, n * NS + 1)
                pe.matmul(bank_flip, mat(FLIP_RE), real_kw[:, 0::2], start=True, stop=False)
                pe.matmul(bank_flip, mat(FLIP_IM), real_kw[:, 1::2], start=False, stop=True).then_inc(flip_done, 1)

            def stage_e(n, q):
                if q == 0:
                    pe.wait_ge(shrunk, n * NS + NS)
                    pe.wait_ge(flip_copied, n + 1)
                for i in range(CHUNK):
                    last = pe.matmul(bank_e(q)[:, :, i], U[:, 0:SIZE, q * CHUNK + i], mat(IH), start=True, stop=True)
                last.then_inc(e_done, 1)

            def stage_f(n, q):
                pe.wait_ge(low_copied, n * NQ + (q + 1))
                for j, (lo, hi) in enumerate(F_SLOTS):
                    k = q * FQ + j
                    if k == NF - 1:
                        pe.wait_ge(f_added, n * NF + (NF - 5))
                    elif k >= len(F_BANKS) and k not in F_LAST:
                        pe.wait_ge(f_added, n * NF + (k - len(F_BANKS) + 1))
                    high, low = sums_high[:, q % RING, lo:hi], sums_low[:, q % RING, lo:hi]
                    pe.matmul(bank_f(q, j), iw_high[:, j], high, start=True, stop=False)
                    pe.matmul(bank_f(q, j), iw_high[:, j], low, start=False, stop=False)
                    pe.matmul(bank_f(q, j), iw_low[:, j], high, start=False, stop=True).then_inc(f_done, 1)

            pe.wait_ge(iw_split, 2)
            pe.wait_ge(mats_loaded, 16)
            pe.wait_ge(padding_set, 4)
            with pe.Fori(0, PAIRS) as m:
                for par in range(2):
                    n = m * 2 + par
                    stage_a(m, par, n, AHEAD * par, NA)
                    for s in range(NS + 2):
                        if s < NS:
                            stage_b(par, n, s)
                        if 1 <= s <= NS:
                            stage_c(n, s - 1)
                        if s >= 2:
                            stage_d(par, n, s - 2)
                    flip(n)
                    if par == 0:
                        stage_a(m, 1, n + 1, 0, AHEAD)
                    for q in range(NQ + LAG):
                        if q < NQ:
                            stage_e(n, q)
                        if q >= LAG:
                            stage_f(n, q - LAG)


INPUTS = ["x", "L0_conv_w1", "L0_conv_b1", "L0_conv_w2", "L0_conv_b2"]


def kernel(**inputs):
    import concourse.bacc as bacc
    from concourse.bass_utils import run_bass_kernel_spmd

    nc = bacc.Bacc("TRN2", target_bir_lowering=False, num_devices=1)
    arrays = {name: np.ascontiguousarray(inputs[name]) for name in INPUTS}
    arrays["dft"] = constants()
    args = [nc.dram_tensor(name, a.shape, F32, kind="ExternalInput").ap() for name, a in arrays.items()]
    out = nc.dram_tensor("out", arrays["x"].shape, F32, kind="ExternalOutput").ap()
    fourier_mlp(nc, *args, out)
    result = run_bass_kernel_spmd(nc, [arrays], core_ids=[0])
    return result.results[0]["out"]
```
